# Optimizing a Trainium2 kernel written in Bass

```python
import numpy as np
import jax
import jax.numpy as jnp

def _softmax(x, axis=-1):
    return jax.nn.softmax(x, axis=axis)

def _gelu(x):
    return jax.nn.gelu(x, approximate=True)

def _silu(x):
    return jax.nn.silu(x)

def _sigmoid(x):
    return jax.nn.sigmoid(x)

def _layernorm(x, axis=-1, eps=1e-05):
    m = jnp.mean(x, axis=axis, keepdims=True)
    v = jnp.var(x, axis=axis, keepdims=True)
    return (x - m) / jnp.sqrt(v + eps)

def _scatter_add(tgt, idx, src, axis=0):
    return tgt.at[idx].add(src)

def _segment_sum(src, seg, n):
    return jax.ops.segment_sum(src, seg, n)
kernel_name = 'mk_gnn_preln_d1_gnn_r8_25a263'

def setup_inputs(seed: int=0):
    np.random.seed(seed)
    _w = jnp.asarray

    def _rec_inputs():
        import jax
        import jax.numpy as jnp
        _gk = jax.random.key(seed)
        x = -0.0001006 + 1 * jax.random.normal(jax.random.fold_in(_gk, 1), (6250, 96), jnp.float32)
        _s = jax.random.randint(jax.random.fold_in(_gk, 2), (100000,), 0, 6250, jnp.int32)
        _d = jax.random.randint(jax.random.fold_in(_gk, 3), (100000,), 0, 6250, jnp.int32)
        _loop = jnp.arange(6250, dtype=jnp.int32)
        src = jnp.concatenate([_s, _d, _loop])
        dst = jnp.concatenate([_d, _s, _loop])
        _o = jnp.argsort(dst, stable=True)
        src = src[_o]
        dst = dst[_o]
        edge_attr_96 = -4.21973e-05 + 0.999841 * jax.random.normal(jax.random.fold_in(_gk, 12), (206250, 96), jnp.float32)
        return (x, src, dst, edge_attr_96)
    x, src, dst, edge_attr_96 = _rec_inputs()

    def _L0_gnn_setup():
        import jax, jax.numpy as jnp
        import numpy as np
        N_NODES = 6250
        N_EDGES = 100000
        EMB = 96
        HID = 2 * EMB
        key = jax.random.key(seed)
        ks = jax.random.split(key, 8)
        h = jax.random.normal(ks[0], (N_NODES, EMB), dtype=jnp.float32)
        edge_attr = jax.random.normal(ks[1], (N_EDGES, EMB), dtype=jnp.float32)
        src = jax.random.randint(ks[2], (N_EDGES,), 0, N_NODES, dtype=jnp.int32)
        dst = jax.random.randint(ks[3], (N_EDGES,), 0, N_NODES, dtype=jnp.int32)
        W1 = jax.random.normal(ks[4], (EMB, HID), dtype=jnp.float32) * (1.0 / np.sqrt(EMB))
        b1 = jnp.zeros((HID,), dtype=jnp.float32)
        W2 = jax.random.normal(ks[5], (HID, EMB), dtype=jnp.float32) * (1.0 / np.sqrt(HID))
        b2 = jnp.zeros((EMB,), dtype=jnp.float32)
        eps = jnp.zeros((1,), dtype=jnp.float32)
        return {'h': h, 'edge_attr': edge_attr, 'src': src, 'dst': dst, 'W1': W1, 'b1': b1, 'W2': W2, 'b2': b2, 'eps': eps}
    _L0_gnn_all = _L0_gnn_setup()
    _L0_gnn_in = {k: v for k, v in _L0_gnn_all.items() if k in ('W1', 'b1', 'W2', 'b2', 'eps')}
    del _L0_gnn_all
    return {'x': x, 'src': src, 'dst': dst, 'edge_attr_96': edge_attr_96, 'L0_gnn_W1': _L0_gnn_in['W1'], 'L0_gnn_b1': _L0_gnn_in['b1'], 'L0_gnn_W2': _L0_gnn_in['W2'], 'L0_gnn_b2': _L0_gnn_in['b2'], 'L0_gnn_eps': _L0_gnn_in['eps']}

def reference(x, src, dst, edge_attr_96, L0_gnn_W1, L0_gnn_b1, L0_gnn_W2, L0_gnn_b2, L0_gnn_eps):
    import jax
    import jax.numpy as jnp

    def _L0_gnn_ref(h, edge_attr, src, dst, W1, b1, W2, b2, eps):
        import jax, jax.numpy as jnp
        import numpy as np
        N_NODES = 6250
        N_EDGES = 100000
        EMB = 96
        HID = 2 * EMB
        m = h[src] + edge_attr
        aggr = jax.ops.segment_sum(m, dst, num_segments=N_NODES)
        hidden = jax.nn.relu(aggr @ W1 + b1)
        mlp_out = hidden @ W2 + b2
        out = (1.0 + eps[0]) * h + mlp_out
        return out
    h = jnp.maximum(_layernorm(x, axis=-1), 0.0)
    x = x + _L0_gnn_ref(h, edge_attr_96, src, dst, L0_gnn_W1, L0_gnn_b1, L0_gnn_W2, L0_gnn_b2, L0_gnn_eps)
    return x

_drawn_inputs = setup_inputs


def setup_inputs(seed=0):
    import zlib

    import numpy as np

    out = dict(_drawn_inputs(seed))
    spreads = {'L0_gnn_b1': (0.0, 0.8), 'L0_gnn_b2': (0.0, 0.8)}
    factors = {}
    for name, (base, spread) in spreads.items():
        noise = np.random.default_rng([zlib.crc32(name.encode()), seed]).standard_normal(out[name].shape)
        drawn = base * np.exp(spread * noise) if base else spread * noise
        out[name] = jnp.asarray(drawn.astype(out[name].dtype))
    for name, factor in factors.items():
        out[name] = (out[name] * factor).astype(out[name].dtype)
    return out
```

```python
from contextlib import ExitStack

import concourse.bass as bass
from concourse import mybir

F32 = mybir.dt.float32
I32 = mybir.dt.int32
F16 = mybir.dt.float16
ALU = mybir.AluOpType
ACT = mybir.ActivationFunctionType
AX_X = mybir.AxisListType.X

P = 128
W = 64
CHUNKS = (10, 10, 9)
TILES = sum(CHUNKS)
BUFS = 4
BLOCK = 512
ADJ_CHUNKS = 2
ADJ = sum(CHUNKS[:ADJ_CHUNKS])
SLOTS = 6
PAIRS = ADJ // 2
AHEAD = 5
assert PAIRS % AHEAD == 0
SPREAD = 128
STEPS = -(-SPREAD // SLOTS)
SCALE = 4096.0


def build(nc, x, src, dst, edge, w1, b1, w2, b2, eps, out):
    N, C = x.shape
    E = src.shape[0]
    H = w1.shape[1] // C
    NT = -(-N // P)
    NLAST = N - (NT - 1) * P
    NC = len(CHUNKS)
    SUPER = P * TILES
    S = -(-E // SUPER)
    FIRST = E - (S - 1) * SUPER
    assert S % BUFS == 0 and S <= P
    COL = [sum(CHUNKS[:c]) for c in range(NC)]
    SHORT = []
    left = FIRST
    for t in CHUNKS:
        n = min(left, P * t)
        assert n % t == 0
        SHORT.append(n // t)
        left -= n
    NTAB = NC + 2
    SPREADS = -(-N // SPREAD)
    MAXW = -(-N // W) + 1
    MAXR = SPREADS * STEPS
    ZC = NT * SLOTS
    NS = ADJ * SLOTS
    AE = P * ADJ
    TURNS = S // BUFS
    PER = 8
    GROUPS = -(-ADJ // PER)
    NB = N // BLOCK
    G = BLOCK // P
    assert NB % 2 == 0 and NB * G == NT - 1

    with ExitStack() as ctx:
        def sb(name, shape, dt=F32):
            return ctx.enter_context(nc.sbuf_tensor(name, shape, dt))

        def pb(name, shape, dt=F32):
            return ctx.enter_context(nc.psum_tensor(name, shape, dt))

        def sem(name):
            return ctx.enter_context(nc.semaphore(name))

        h_dram = nc.dram_tensor("h_rows", [N, C], F32).ap()
        tab_dram = nc.dram_tensor("window_table", [S, NTAB], I32).ap()

        slot_dram = nc.dram_tensor("tile_offsets", [S, ADJ], F32).ap()

        x_sb = sb("x_sb", [P, NT, C])
        h_sb = sb("h_sb", [P, NT, C])
        hl = sb("hl", [P, NT, 2 * C], F16)
        stat = sb("stat", [P, NT])
        rstd = sb("rstd", [P, NT])
        acc = sb("acc", [P, N + SPREAD])
        accT = acc[0:C, :]
        adj_words = sb("adj_words", [P, 2, NT * NS // 2])
        adj = [adj_words[:, k, :].bitcast(F16).rearrange("p (h n) -> p h n", n=NS) for k in range(2)]
        edges = [sb(f"edges{k}", [P, TILES, C]) for k in range(BUFS)]
        tmp = adj_words[:, :, :].rearrange("p k n -> p (k n)")[:, 0:NT * C].rearrange("p (t c) -> p t c", c=C)
        dstT = acc[0:S, 0:SUPER].bitcast(I32)
        srcT = acc[0:S, SUPER:SUPER + AE].bitcast(I32)
        relT = edges[3][0:S, :, :].rearrange("p t c -> p (t c)")[:, 0:AE]
        srcF = edges[2][0:S, :, :].rearrange("p t c -> p (t c)")[:, 0:AE]
        tmin = sb("tmin", [S, ADJ])
        tmax = sb("tmax", [S, ADJ])
        slotT = sb("slotT", [S, ADJ, SLOTS])
        cmax = sb("cmax", [S, NTAB])
        cmin = sb("cmin", [S, NTAB])
        span = sb("span", [S, NTAB])
        need = sb("need", [S, 6], I32)
        needf = sb("needf", [S, 6])
        tabT = sb("tabT", [S, NTAB], I32)
        tab = sb("tab", [P, S * NTAB], I32)
        tabf = sb("tabf", [P, S * NTAB])
        offs = sb("offs", [P, S * ADJ])
        key_lo = sb("key_lo", [P, 2, ADJ, S])
        key, lo = key_lo[:, 0, :, :], key_lo[:, 1, :, :]
        now = [sb(f"now{k}", [P, 2, ADJ]) for k in range(2)]
        rel_adj = sb("rel_adj", [P, ADJ, S])
        hi = sb("hi", [P, ADJ, S])
        src_i = sb("src_i", [P, ADJ, S], I32)
        slot_node = sb("slot_node", [NS, S])
        slot_tile = sb("slot_tile", [NS, S])
        slot_place = sb("slot_place", [NS, 1])
        place_row = sb("place_row", [1, ADJ, SLOTS])
        iota_i = sb("iota_i", [P, ZC], I32)
        iota_w = sb("iota_w", [P, SPREAD])
        iota_z = sb("iota_z", [P, ZC], F16)
        ident_i = sb("ident_i", [P, P], I32)
        ident = sb("ident", [P, P])
        step_i = sb("step_i", [P, SPREADS + STEPS + MAXW], I32)
        step_f = sb("step_f", [P, SPREADS + STEPS + MAXW])
        src_sb = [sb(f"src{k}", [P, TILES], I32) for k in range(BUFS)]
        dst_sb = [sb(f"dst{k}", [P, TILES], I32) for k in range(BUFS)]
        rel = [sb(f"rel{k}", [P, TILES]) for k in range(2)]
        hot = [sb(f"hot{k}", [P, TILES, W]) for k in range(2)]
        z = [sb(f"z{k}", [P, 2, ZC], F16) for k in range(AHEAD - 2)]
        z_home = src_i[:, :, :].bitcast(F16).rearrange("p t s -> p (t s)")
        z += [z_home[:, 2 * ZC * k:2 * ZC * (k + 1)].rearrange("p (i n) -> p i n", i=2) for k in range(3)]
        lo_hot = [sb(f"lo_hot{k}", [P, 2, P], F16) for k in range(AHEAD)]
        lo_hot.append(z_home[:, 6 * ZC:6 * ZC + 2 * P].rearrange("p (i n) -> p i n", i=2))
        slot_half = sb("slot_half", [NS, C])
        slot_sum = sb("slot_sum", [NS, C])
        slot_id = sb("slot_id", [NS, 2])
        slot_hot = sb("slot_hot", [NS, SPREAD])
        xkey = sb("xkey", [P, 4, ADJ])
        w1_sb = sb("w1_sb", [C, H, C])
        w2_sb = sb("w2_sb", [C, H, C])
        b1_sb = sb("b1_sb", [C, H])
        b2_sb = sb("b2_sb", [P, C])
        eps_sb = sb("eps_sb", [P, 1])
        hid = [hot[k][0:C, :, :].rearrange("p t w -> p (t w)")[:, 0:H * BLOCK].rearrange("p (j n) -> p j n", j=H) for k in range(2)]

        seg = [pb(f"seg{k}", [P, 512]) for k in range(2)]
        pair_ps = pb("pair_ps", [P, 4, 512])
        slots_ps = pb("slots_ps", [P, 512])
        spread_ps = pb("spread_ps", [P, 512])
        xseg_ps, xspread_ps = pair_ps[:, 2, :], pair_ps[:, 3, :]
        hid_ps = [pair_ps[:, j, :] for j in range(H)]
        out_ps = [pair_ps[:, H + j, :] for j in range(2)]

        x_clear = sem("x_clear")
        x_in = sem("x_in")
        w_in = sem("w_in")
        dstT_in = sem("dstT_in")
        dve = sem("dve_chain")
        var_ready = sem("var_ready")
        std_ready = sem("std_ready")
        h_ready = sem("h_ready")
        h_stored = sem("h_stored")
        tab_ready = sem("tab_ready")
        tab_stored = sem("tab_stored")
        tab_in = sem("tab_in")
        tabf_ready = sem("tabf_ready")
        iotas = sem("iotas")
        consts = sem("consts")
        buf_clear = sem("buf_clear")
        edges_in = [sem(f"edges_in{k}") for k in range(BUFS)]
        ids_in = [sem(f"ids_in{k}") for k in range(BUFS)]
        gathered = [sem(f"gathered{k}") for k in range(BUFS)]
        rel_ready = sem("rel_ready")
        hot_ready = sem("hot_ready")
        seg_done = sem("seg_done")
        seg_added = sem("seg_added")
        xrel_ready = sem("xrel_ready")
        xhot_ready = sem("xhot_ready")
        xseg_done = sem("xseg_done")
        xseg_added = sem("xseg_added")
        srcT_in = sem("srcT_in")
        offs_in = sem("offs_in")
        offs_stored = sem("offs_stored")
        offs_ready = sem("offs_ready")
        rel_T_ready = sem("rel_T_ready")
        turned = sem("turned")
        turn_read = sem("turn_read")
        keys_ready = sem("keys_ready")
        now_ready = sem("now_ready")
        z_ready = sem("z_ready")
        pair_done = sem("pair_done")
        pair_read = sem("pair_read")
        slots_done = sem("slots_done")
        half_ready = sem("half_ready")
        slot_id_ready = sem("slot_id_ready")
        slots_ready = sem("slots_ready")
        spread_done = sem("spread_done")
        xz_ready = sem("xz_ready")
        xkey_ready = sem("xkey_ready")
        xpair_done = sem("xpair_done")
        xpair_read = sem("xpair_read")
        xslots_done = sem("xslots_done")
        xhalf_ready = sem("xhalf_ready")
        xslot_id_ready = sem("xslot_id_ready")
        xslots_ready = sem("xslots_ready")
        xspread_done = sem("xspread_done")
        hl_ready = sem("hl_ready")
        agg_ready = sem("agg_ready")
        hid_done = sem("hid_done")
        hid_ready = sem("hid_ready")
        out_done = sem("out_done")
        out_ready = sem("out_ready")
        out_stored = sem("out_stored")

        def start_of(s):
            return FIRST + (s - 1) * SUPER

        block = ctx.enter_context(nc.Block())

        @block.sync
        def _(sp):
            sp.wait_ge(x_clear, 1)
            sp.dma_start(x_sb[:, 0:NT - 1, :], x[0:(NT - 1) * P, :].rearrange("(t p) c -> p t c", p=P)).then_inc(x_in, 16)
            sp.dma_start(x_sb[0:NLAST, NT - 1, :], x[(NT - 1) * P:N, :]).then_inc(x_in, 16)
            with nc.allow_non_contiguous_dma(reason="bias of 192 values to columns"):
                sp.dma_start(b1_sb[:, :], b1.rearrange("(j c) -> c j", c=C)).then_inc(w_in, 16)
            sp.dma_start(w1_sb[:, :, :], w1.rearrange("k (j c) -> k j c", c=C)).then_inc(w_in, 16)
            sp.dma_start(w2_sb[:, :, :], w2.rearrange("(j k) c -> k j c", k=C)).then_inc(w_in, 16)
            sp.dma_start(b2_sb[:, :], b2.partition_broadcast(P)).then_inc(w_in, 16)
            sp.dma_start(eps_sb[:, :], eps.partition_broadcast(P)).then_inc(w_in, 16)
            sp.dma_start(dstT[0:1, :], dst[0:SUPER].rearrange("(s e) -> s e", s=1)).then_inc(dstT_in, 16)
            sp.dma_start(dstT[1:S, :], dst[FIRST:E].rearrange("(s e) -> s e", e=SUPER)).then_inc(dstT_in, 16)

            def load(k, s, short=False):
                for c in range(NC):
                    t, a = CHUNKS[c], COL[c]
                    rows = SHORT[c] if short else P
                    if not rows:
                        continue
                    n = 16 if not short or any(SHORT[c + 1:]) else 16 * (NC - c)
                    e0 = P * a if short else start_of(s) + P * a
                    def cut(v):
                        return v[bass.ds(e0, rows * t)] if not isinstance(e0, int) else v[e0:e0 + rows * t]
                    sp.dma_start(src_sb[k][0:rows, a:a + t], cut(src).rearrange("(p t) -> p t", t=t)).then_inc(ids_in[k], n)
                    sp.dma_start(dst_sb[k][0:rows, a:a + t], cut(dst).rearrange("(p t) -> p t", t=t)).then_inc(ids_in[k], n)
                    ev = edge[bass.ds(e0, rows * t), :] if not isinstance(e0, int) else edge[e0:e0 + rows * t, :]
                    sp.dma_start(edges[k][0:rows, a:a + t, :], ev.rearrange("(p t) c -> p t c", t=t)).then_inc(edges_in[k], n)

            sp.dma_start(srcT[0:1, :], src[0:AE].rearrange("(s e) -> s e", s=1)).then_inc(srcT_in, 16)
            sp.dma_start(srcT[1:S, :], src[FIRST:E].rearrange("(s e) -> s e", e=SUPER)[:, 0:AE]).then_inc(srcT_in, 16)
            sp.wait_ge(buf_clear, 3)
            load(0, 0, short=True)
            load(1, 1)
            sp.wait_ge(tab_ready, 1)
            sp.dma_start(tab_dram, tabT[:, :]).then_inc(tab_stored, 16)
            sp.wait_ge(tab_stored, 16)
            sp.dma_start(tab[:, :], tab_dram.rearrange("s n -> (s n)").partition_broadcast(P)).then_inc(tab_in, 16)
            sp.wait_ge(offs_ready, 1)
            sp.dma_start(slot_dram, tmin[:, :]).then_inc(offs_stored, 16)
            sp.wait_ge(offs_stored, 16)
            sp.dma_start(offs[:, :], slot_dram.rearrange("s n -> (s n)").partition_broadcast(P)).then_inc(offs_in, 16)
            sp.wait_ge(h_ready, 1)
            sp.dma_start(h_dram[0:(NT - 1) * P, :].rearrange("(t p) c -> p t c", p=P), h_sb[:, 0:NT - 1, :]).then_inc(h_stored, 16)
            sp.dma_start(h_dram[(NT - 1) * P:N, :], h_sb[0:NLAST, NT - 1, :]).then_inc(h_stored, 16)
            sp.wait_ge(turned, 2 * GROUPS)
            for k in range(2, BUFS):
                load(k, k)
            with sp.Fori(1, TURNS) as turn:
                for k in range(BUFS):
                    s = turn * BUFS + k
                    sp.wait_ge(seg_done, s - BUFS + 2)
                    load(k, s)
            for i in range(NT // 4):
                sp.wait_ge(out_ready, 4 * (i + 1))
                sp.dma_start(out[i * BLOCK:(i + 1) * BLOCK, :].rearrange("(t p) c -> p t c", p=P),
                             x_sb[:, 4 * i:4 * i + 4, :]).then_inc(out_stored, 16)
            sp.wait_ge(out_ready, NT)
            sp.dma_start(out[(NT - 1) * P:N, :], x_sb[0:NLAST, NT - 1, :]).then_inc(out_stored, 16)
            sp.wait_ge(out_stored, 16 * (NT // 4 + 1))

        @block.gpsimd
        def _(pool):
            nc.gpsimd.iota(iota_i[:, :], [[1, ZC]], base=0, channel_multiplier=0).then_inc(iotas, 1)
            nc.gpsimd.iota(ident_i[:, :], [[1, P]], base=0, channel_multiplier=-1).then_inc(iotas, 1)
            nc.gpsimd.iota(step_i[:, 0:SPREADS], [[SPREAD, SPREADS]], base=0, channel_multiplier=0).then_inc(iotas, 1)
            nc.gpsimd.iota(step_i[:, SPREADS:SPREADS + STEPS], [[SLOTS, STEPS]], base=0, channel_multiplier=0).then_inc(iotas, 1)
            nc.gpsimd.iota(step_i[:, SPREADS + STEPS:], [[W, MAXW]], base=0, channel_multiplier=0).then_inc(iotas, 1)
            nc.gpsimd.memset(src_sb[0][:, :], 0).then_inc(buf_clear, 1)
            nc.gpsimd.memset(dst_sb[0][:, :], -1).then_inc(buf_clear, 1)
            nc.gpsimd.memset(edges[0][:, :, :], 0.0).then_inc(buf_clear, 1)
            ids = pool.alloc_register("ids_loaded")
            rows = pool.alloc_register("edges_loaded")
            with pool.Fori(0, TURNS) as turn:
                for k in range(BUFS):
                    pool.reg_mov(ids, (turn + 1) * (32 * NC))
                    pool.reg_mov(rows, (turn + 1) * (16 * NC))
                    pool.wait_ge(h_stored, 32)
                    pool.wait_ge(ids_in[k], ids)
                    pool.wait_ge(edges_in[k], rows)
                    for t in range(ADJ, TILES):
                        nc.gpsimd.indirect_dma_start(
                            out=edges[k][:, t, :], out_offset=None, in_=h_dram[:, :],
                            in_offset=bass.IndirectOffsetOnAxis(ap=src_sb[k][:, t:t + 1], axis=0),
                            compute_op=ALU.add).then_inc(gathered[k], 16)

        @block.vector
        def _(v):
            link = [0]

            def chain(ins):
                link[0] += 1
                ins.then_inc(dve, 1)
                v.wait_ge(dve, link[0])

            nc.vector.memset(x_sb[:, NT - 1, :], 0.0).then_inc(x_clear, 1)
            v.wait_ge(iotas, 5)
            nc.vector.tensor_copy(iota_w[:, :], iota_i[:, 0:SPREAD])
            nc.vector.tensor_copy(iota_z[:, :], iota_i[:, :])
            nc.vector.tensor_scalar(ident[:, :], ident_i[:, :], 0.0, None, ALU.is_equal)
            nc.vector.tensor_copy(place_row[:, :, :], iota_i[0:1, 0:SLOTS].rearrange("p (o q) -> p o q", o=1).broadcast_to([1, ADJ, SLOTS]))
            nc.vector.tensor_copy(step_f[:, :], step_i[:, :]).then_inc(consts, 1)
            v.wait_ge(consts, 1)
            v.wait_ge(dstT_in, 32)
            tiles = dstT[:, 0:AE].rearrange("s (t e) -> s t e", e=P)
            nc.vector.tensor_reduce(tmin[:, :], tiles, AX_X, ALU.min)
            chain(nc.vector.tensor_reduce(tmax[:, :], tiles, AX_X, ALU.max))
            for c in range(ADJ_CHUNKS):
                sl = slice(COL[c], COL[c] + CHUNKS[c])
                nc.vector.tensor_reduce(cmin[:, c:c + 1], tmin[:, sl], AX_X, ALU.min)
                nc.vector.tensor_reduce(cmax[:, c:c + 1], tmax[:, sl], AX_X, ALU.max)
            nc.vector.tensor_reduce(cmin[:, NC - 1:NC], dstT[:, AE:SUPER], AX_X, ALU.min)
            nc.vector.tensor_reduce(cmax[:, NC - 1:NC], dstT[:, AE:SUPER], AX_X, ALU.max)
            nc.vector.tensor_reduce(cmin[:, NC:NC + 1], tmin[:, :], AX_X, ALU.min)
            nc.vector.tensor_reduce(cmax[:, NC:NC + 1], tmax[:, :], AX_X, ALU.max)
            chain(nc.vector.tensor_tensor(relT.rearrange("s (t e) -> s t e", e=P), tiles,
                                          tmin[:, :].rearrange("s (t o) -> s t o", o=1).broadcast_to([S, ADJ, P]), ALU.subtract))
            nc.vector.memset(relT[0:1, FIRST:AE], -1.0)
            chain(nc.vector.tensor_tensor(span[:, 0:NC + 1], cmax[:, 0:NC + 1], cmin[:, 0:NC + 1], ALU.subtract))
            v.wait_ge(srcT_in, 32)
            nc.vector.tensor_copy(srcF, srcT).then_inc(rel_T_ready, 1)
            chain(nc.vector.tensor_reduce(need[:, 0:1], span[:, 0:NC], AX_X, ALU.max))
            chain(nc.vector.tensor_scalar(need[:, 0:1], need[:, 0:1], 6, None, ALU.arith_shift_right))
            chain(nc.vector.tensor_copy(need[:, 1:2], span[:, NC:NC + 1]))
            chain(nc.vector.tensor_scalar(need[:, 1:2], need[:, 1:2], 7, None, ALU.arith_shift_right))
            chain(nc.vector.tensor_tensor(tmax[:, :], tmax[:, :], tmin[:, :], ALU.subtract))
            chain(nc.vector.tensor_reduce(needf[:, 0:1], tmax[:, :], AX_X, ALU.max))
            chain(nc.vector.tensor_scalar(need[:, 2:3], needf[:, 0:1], float(SPREAD - 1), 171.0, ALU.min, ALU.mult))
            chain(nc.vector.tensor_scalar(need[:, 2:3], need[:, 2:3], 10, None, ALU.arith_shift_right))
            chain(nc.vector.tensor_copy(needf[:, 0:3], need[:, 0:3]))
            chain(nc.vector.tensor_scalar(needf[:, 3:4], needf[:, 1:2], 1.0, float(STEPS), ALU.add, ALU.mult))
            chain(nc.vector.tensor_scalar(needf[:, 4:5], needf[:, 1:2], 0.0, None, ALU.is_gt))
            chain(nc.vector.tensor_scalar(needf[:, 3:4], needf[:, 3:4], 1.0, None, ALU.subtract))
            chain(nc.vector.tensor_tensor(needf[:, 3:4], needf[:, 3:4], needf[:, 4:5], ALU.mult))
            chain(nc.vector.tensor_tensor(needf[:, 0:1], needf[:, 0:1], needf[:, 2:3], ALU.max))
            chain(nc.vector.tensor_tensor(needf[:, 0:1], needf[:, 0:1], needf[:, 3:4], ALU.max))
            nc.vector.tensor_copy(tabT[:, 0:NC], cmin[:, 0:NC])
            nc.vector.tensor_copy(tabT[:, NC + 1:NC + 2], cmin[:, NC:NC + 1])
            nc.vector.tensor_scalar(tabT[:, NC:NC + 1], needf[:, 0:1], 1.0, None, ALU.add).then_inc(tab_ready, 1)
            chain(nc.vector.tensor_scalar(tmin[:, :], tmin[:, :], cmin[:, NC:NC + 1], None, ALU.subtract))
            nc.vector.tensor_copy(slotT[:, :, :], tmin[:, :].rearrange("s (t o) -> s t o", o=1).broadcast_to([S, ADJ, SLOTS])).then_inc(offs_ready, 1)
            v.wait_ge(x_in, 32)
            def wide(a):
                return a.rearrange("p (t o) -> p t o", o=1).broadcast_to([P, NT, C])
            chain(nc.vector.tensor_reduce(stat[:, :], x_sb[:, :, :], AX_X, ALU.add))
            chain(nc.vector.tensor_scalar(stat[:, :], stat[:, :], 1.0 / C, None, ALU.mult))
            chain(nc.vector.tensor_tensor(h_sb[:, :, :], x_sb[:, :, :], wide(stat[:, :]), ALU.subtract))
            chain(nc.vector.tensor_tensor(tmp[:, :, :], h_sb[:, :, :], h_sb[:, :, :], ALU.mult))
            chain(nc.vector.tensor_reduce(stat[:, :], tmp[:, :, :], AX_X, ALU.add))
            nc.vector.tensor_scalar(stat[:, :], stat[:, :], 1.0 / C, 1e-5, ALU.mult, ALU.add).then_inc(var_ready, 1)
            v.wait_ge(std_ready, 1)
            chain(nc.vector.reciprocal(rstd[:, :], rstd[:, :]))
            chain(nc.vector.tensor_tensor(h_sb[:, :, :], h_sb[:, :, :], wide(rstd[:, :]), ALU.mult))
            chain(nc.vector.tensor_scalar(h_sb[:, :, :], h_sb[:, :, :], 0.0, None, ALU.max))
            nc.vector.tensor_scalar(h_sb[:, :, :], h_sb[:, :, :], 0.0, None, ALU.max).then_inc(h_ready, 1)
            v.wait_ge(h_ready, 1)
            chain(nc.vector.tensor_scalar(tmp, h_sb[:, :, :], SCALE, None, ALU.mult))
            chain(nc.vector.tensor_copy(hl[:, :, 0:C], tmp))
            nc.vector.tensor_tensor(hl[:, :, C:2 * C], tmp, hl[:, :, 0:C], ALU.subtract).then_inc(hl_ready, 1)
            v.wait_ge(hl_ready, 1)
            v.wait_ge(w_in, 16 * 5)
            chain(nc.vector.tensor_scalar(eps_sb[:, :], eps_sb[:, :], 1.0, None, ALU.add))
            chain(nc.vector.scalar_tensor_tensor(x_sb[:, :, :], h_sb[:, :, :], eps_sb[:, 0:1], x_sb[:, :, :], ALU.mult, ALU.add))
            chain(nc.vector.tensor_tensor(x_sb[:, :, :], x_sb[:, :, :],
                                          b2_sb[:, :].rearrange("p (o c) -> p o c", o=1).broadcast_to([P, NT, C]), ALU.add))
            v.wait_ge(tab_in, 16)
            nc.vector.tensor_copy(tabf[:, :], tab[:, :]).then_inc(tabf_ready, 1)
            v.wait_ge(tabf_ready, 1)
            v.wait_ge(offs_in, 16)
            for n in range(GROUPS):
                a, b = n * PER, min(ADJ, (n + 1) * PER)
                width = (b - a) * S
                v.wait_ge(turned, 2 * n + 2)
                nc.vector.tensor_copy(rel_adj[:, a:b, :].rearrange("p t s -> p (t s)"), pair_ps[:, 0, 0:width])
                nc.vector.tensor_copy(src_i[:, a:b, :].rearrange("p t s -> p (t s)"), pair_ps[:, 1, 0:width]).then_inc(turn_read, 1)
                v.wait_ge(turn_read, n + 1)
            v.wait_ge(turned, 2 * GROUPS + 1)
            chain(nc.vector.tensor_copy(slot_tile[:, :], slots_ps[0:NS, 0:S]))
            chain(nc.vector.tensor_copy(slot_place[:, :], spread_ps[0:NS, 0:1]))
            chain(nc.vector.tensor_scalar(slot_node[:, :], slot_tile[:, :], slot_place[:, 0:1], None, ALU.add))
            lo_i = lo[:, :, :].bitcast(I32)
            hi_i = hi[:, :, :].bitcast(I32)
            chain(nc.vector.tensor_scalar(hi_i, src_i[:, :, :], 7, None, ALU.logical_shift_right))
            chain(nc.vector.tensor_scalar(lo_i, src_i[:, :, :], P - 1, None, ALU.bitwise_and))
            chain(nc.vector.tensor_copy(src_i[:, :, :].bitcast(F32), hi_i))
            chain(nc.vector.tensor_scalar(hi[:, :, :], src_i[:, :, :].bitcast(F32), float(SLOTS), None, ALU.mult))
            chain(nc.vector.tensor_copy(src_i[:, :, :].bitcast(F32), lo_i))
            chain(nc.vector.tensor_copy(lo[:, :, :], src_i[:, :, :].bitcast(F32)))

            def keys(out, t, r, h, link_after):
                link_after(nc.vector.scalar_tensor_tensor(t, h, 1.0, r, ALU.add, ALU.add))
                link_after(nc.vector.scalar_tensor_tensor(t, r, 0.0, t, ALU.is_ge, ALU.mult))
                link_after(nc.vector.scalar_tensor_tensor(t, r, float(SLOTS), t, ALU.is_lt, ALU.mult))
                return nc.vector.tensor_scalar(out, t, 1.0, None, ALU.subtract)

            keys(key[:, :, :], src_i[:, :, :].bitcast(F32), rel_adj[:, :, :], hi[:, :, :], chain).then_inc(keys_ready, 1)
            v.wait_ge(keys_ready, 1)
            chain(nc.vector.memset(acc[:, :], 0.0))
            extra = v.alloc_register("vector_extra_passes")
            v.reg_mov(extra, 0)
            added = v.alloc_register("windows_added")
            at = v.alloc_register("window_column")
            spread_count = v.alloc_register("spreads_done")

            WCOL = SPREADS + STEPS

            def one_hot(k, s, r, rel_sem, rel_value, hot_sem):
                for c in range(NC):
                    a, b = COL[c], COL[c] + CHUNKS[c]
                    last = nc.vector.tensor_scalar(rel[k % 2][:, a:b], dst_sb[k][:, a:b], tabf[:, bass.ds(s * NTAB + c, 1)],
                                                   step_f[:, bass.ds(WCOL + r, 1)], ALU.subtract, ALU.subtract)
                last.then_inc(rel_sem, 1)
                v.wait_ge(rel_sem, rel_value)
                nc.vector.tensor_tensor(
                    hot[k % 2][:, :, :],
                    iota_w[:, 0:W].rearrange("p (o w) -> p o w", o=1).broadcast_to([P, TILES, W]),
                    rel[k % 2][:, :].rearrange("p (t o) -> p t o", o=1).broadcast_to([P, TILES, W]),
                    ALU.is_equal).then_inc(hot_sem, 1)

            spread_at = v.alloc_register("spread_column")

            def window_bases(s):
                return [v.value_load(tab[0:1, bass.ds(s * NTAB + c, 1)], min_val=0, max_val=N - 1) for c in (*range(NC), NC + 1)]

            ADDS = NC + 1

            def add_window(k, base, s, c):
                width, part = (W, seg[k % 2][0:C, W * c:W * (c + 1)]) if c < NC else (SPREAD, spread_ps[0:C, 0:SPREAD])
                if not (isinstance(s, int) and s == 0 and c == 0):
                    v.wait_ge(seg_added, s * ADDS + c)
                sl = accT[:, bass.ds(base, width)]
                nc.vector.tensor_tensor(sl, sl, part, ALU.add).then_inc(seg_added, 1)

            def add_extra(k, bases, r, before):
                for c in range(ADDS):
                    width, part = (W, xseg_ps[0:C, W * c:W * (c + 1)]) if c < NC else (SPREAD, xspread_ps[0:C, 0:SPREAD])
                    v.reg_mov(at, bases[c] + (r * W if c < NC else (r // STEPS) * SPREAD))
                    v.reg_alu(at, at, N, ALU.min)
                    sl = accT[:, bass.ds(v.snap(at, min_val=0, max_val=N), width)]
                    v.reg_mov(added, before * ADDS + (c + 1))
                    nc.vector.tensor_tensor(sl, sl, part, ALU.add).then_inc(xseg_added, 1)
                    v.wait_ge(tabf_ready, 1)
                    v.wait_ge(xseg_added, added)

            def build_pair(buf, g, column, low, ready):
                for i in (0, 1):
                    nc.vector.tensor_scalar(z[buf][:, i, :], iota_z[:, :], column(2 * g + i), None, ALU.is_equal)
                    last = nc.vector.tensor_scalar(lo_hot[buf][:, i, :], iota_z[:, 0:P], low(2 * g + i), None, ALU.is_equal)
                last.then_inc(ready, 1)

            def take_columns(k, s):
                nc.vector.tensor_copy(now[k % 2][:, :, :].rearrange("p a t -> p (a t)"),
                                      key_lo[:, :, :, bass.ds(s, 1)].rearrange("p a t o -> p (a t o)")).then_inc(now_ready, 1)
                v.wait_ge(now_ready, s + 1)

            def main_pair(k, s, g):
                if not (isinstance(s, int) and s * PAIRS + g < AHEAD):
                    v.wait_ge(pair_done, s * PAIRS + (g + 1 - AHEAD))
                build_pair(g % AHEAD, g, lambda t: now[k % 2][:, 0, t:t + 1], lambda t: now[k % 2][:, 1, t:t + 1], z_ready)

            def slots_to_nodes(s, spread, step, id_sem, half_sem, value, ready):
                nc.vector.tensor_scalar(slot_id[:, 0:1], slot_node[:, bass.ds(s, 1)], step_f[0:NS, bass.ds(SPREADS + step, 1)],
                                        step_f[0:NS, bass.ds(spread, 1)], ALU.add, ALU.subtract).then_inc(id_sem, 1)
                v.wait_ge(id_sem, value)
                nc.vector.tensor_scalar(slot_hot[:, :], iota_w[0:NS, :], slot_id[:, 0:1], None, ALU.is_equal)
                v.wait_ge(half_sem, value)
                nc.vector.scalar_tensor_tensor(slot_sum[:, :], slots_ps[0:NS, C:2 * C], 1.0 / SCALE, slot_half[:, :],
                                               ALU.mult, ALU.add).then_inc(ready, 1)

            def build(k, s, turn):
                v.wait_ge(ids_in[k], (turn + 1) * (32 * NC))
                one_hot(k, s, 0, rel_ready, s + 1, hot_ready)

            def finish(k, s):
                passes = v.value_load(tab[0:1, bass.ds(s * NTAB + NC, 1)], min_val=1, max_val=MAXR)
                slots_to_nodes(s, 0, 0, slot_id_ready, half_ready, s + 1, slots_ready)
                with v.If(passes > 1):
                    v.reg_mov(added, s * ADDS if not isinstance(s, int) or s else 0)
                    v.reg_mov(spread_count, s + 1)
                    bases = window_bases(s)
                    v.wait_ge(tabf_ready, 1)
                    v.wait_ge(seg_added, added)
                    v.wait_ge(tabf_ready, 1)
                    v.wait_ge(spread_done, spread_count)
                    with v.Fori(1, passes) as r:
                        n = v.snap(extra, min_val=0, max_val=S * MAXR)
                        v.reg_mov(spread_at, r // STEPS)
                        v.reg_mov(step_at, r % STEPS)
                        spread = v.snap(spread_at, min_val=0, max_val=SPREADS - 1)
                        step = v.snap(step_at, min_val=0, max_val=STEPS - 1)
                        one_hot(k, s, smin_w(r), xrel_ready, n + 1, xhot_ready)
                        extra_keys(s, spread, step, n)
                        for g in range(PAIRS):
                            build_pair(AHEAD, g, lambda t: xkey[:, 3, t:t + 1], lambda t: now[k % 2][:, 1, t:t + 1], xz_ready)
                            v.wait_ge(xpair_read, n * PAIRS + (g + 1))
                        extra_slots(s, spread, step, n)
                        v.wait_ge(xspread_done, n + 1)
                        add_extra(k, bases, r, n)
                        v.reg_add(extra, extra, 1)

            step_at = v.alloc_register("step_column")
            window_at = v.alloc_register("window_pass")

            def smin_w(r):
                v.reg_mov(window_at, r)
                v.reg_alu(window_at, window_at, MAXW - 1, ALU.min)
                return v.snap(window_at, min_val=0, max_val=MAXW - 1)

            def extra_keys(s, spread, step, n):
                count = [0]

                def link_extra(ins):
                    count[0] += 1
                    ins.then_inc(xkey_ready, 1)
                    v.wait_ge(xkey_ready, n * KEY_OPS + count[0])

                tile_at = offs[:, bass.ds(s * ADJ, ADJ)]
                column = step_f[:, bass.ds(spread, 1)]
                link_extra(nc.vector.tensor_scalar(xkey[:, 0, :], tile_at, column, -1.0, ALU.subtract, ALU.mult))
                link_extra(nc.vector.tensor_scalar(xkey[:, 0, :], xkey[:, 0, :], 0.0, step_f[:, bass.ds(SPREADS + step, 1)], ALU.max, ALU.add))
                link_extra(nc.vector.tensor_tensor(xkey[:, 1, :], rel_adj[:, :, bass.ds(s, 1)].rearrange("p t o -> p (t o)"),
                                                   xkey[:, 0, :], ALU.subtract))
                link_extra(keys(xkey[:, 3, :], xkey[:, 2, :], xkey[:, 1, :], hi[:, :, bass.ds(s, 1)].rearrange("p t o -> p (t o)"), link_extra))
                assert count[0] == KEY_OPS

            KEY_OPS = 7

            def extra_slots(s, spread, step, n):
                nc.vector.tensor_scalar(slot_id[:, 1:2], slot_tile[:, bass.ds(s, 1)], step_f[0:NS, bass.ds(spread, 1)], slot_place[:, 0:1],
                                        ALU.max, ALU.add).then_inc(xslot_id_ready, 1)
                v.wait_ge(xslot_id_ready, 3 * n + 1)
                nc.vector.tensor_scalar(slot_id[:, 0:1], slot_id[:, 1:2], step_f[0:NS, bass.ds(SPREADS + step, 1)],
                                        step_f[0:NS, bass.ds(spread, 1)], ALU.add, ALU.subtract).then_inc(xslot_id_ready, 1)
                v.wait_ge(xslot_id_ready, 3 * n + 2)
                nc.vector.tensor_scalar(slot_hot[:, :], iota_w[0:NS, :], slot_id[:, 0:1], None, ALU.is_equal).then_inc(xslot_id_ready, 1)
                v.wait_ge(xhalf_ready, n + 1)
                nc.vector.scalar_tensor_tensor(slot_sum[:, :], slots_ps[0:NS, C:2 * C], 1.0 / SCALE, slot_half[:, :],
                                               ALU.mult, ALU.add).then_inc(xslots_ready, 1)

            def super_chunk(k, s, turn, first, last):
                if not first:
                    bases = window_bases(s - 1)
                for g in range(AHEAD, PAIRS):
                    main_pair(k, s, g)
                    if first:
                        continue
                    if g == AHEAD:
                        v.wait_ge(spread_done, s)
                    if g - AHEAD < ADDS:
                        add_window((k + 1) % 2, bases[g - AHEAD], s - 1, g - AHEAD)
                if not last:
                    build((k + 1) % BUFS, s + 1, turn + (k + 1) // BUFS)
                    take_columns(k + 1, s + 1)
                    for g in range(AHEAD):
                        main_pair(k + 1, s + 1, g)
                finish(k, s)

            build(0, 0, 0)
            take_columns(0, 0)
            for g in range(AHEAD):
                main_pair(0, 0, g)
            for k in range(BUFS):
                super_chunk(k, k, 0, k == 0, False)
            with v.Fori(1, TURNS - 1) as turn:
                for k in range(BUFS):
                    super_chunk(k, turn * BUFS + k, turn, False, False)
            for k in range(BUFS):
                super_chunk(k, S - BUFS + k, TURNS - 1, False, k + 1 == BUFS)
            bases = window_bases(S - 1)
            v.wait_ge(spread_done, S)
            for c in range(ADDS):
                add_window((S - 1) % 2, bases[c], S - 1, c)
            v.wait_ge(seg_added, S * ADDS)
            nc.vector.memset(tmp[0:1, 0, 0:1], 0.0).then_inc(agg_ready, 1)

            def add_residual(tile, n, count):
                v.wait_ge(out_done, count)
                nc.vector.tensor_tensor(x_sb[0:n, bass.ds(tile, 1), :].rearrange("p o c -> p (o c)"),
                                        x_sb[0:n, bass.ds(tile, 1), :].rearrange("p o c -> p (o c)"),
                                        out_ps[n_buf[0] % 2][0:n, 0:C], ALU.add).then_inc(out_ready, 1)
            n_buf = [0]
            with v.Fori(0, NB) as b:
                for g in range(G):
                    n_buf[0] = g
                    add_residual(b * G + g, P, b * G + (g + 1))
            n_buf[0] = 0
            add_residual(NT - 1, NLAST, NT)

        @block.scalar
        def _(act):
            def relu(k, n, b):
                act.wait_ge(hid_done, b + 1)
                for j in range(H):
                    last = nc.scalar.activation(hid[k][:, j, 0:n], hid_ps[j][0:C, 0:n], ACT.Relu, bias=b1_sb[:, j:j + 1])
                last.then_inc(hid_ready, 1)

            act.wait_ge(var_ready, 1)
            nc.scalar.activation(rstd[:, :], stat[:, :], ACT.Sqrt).then_inc(std_ready, 1)
            def read_pair(k, bank, g):
                a = 2 * g * SLOTS
                return nc.scalar.activation(
                    adj[k % 2][:, :, a:a + 2 * SLOTS].rearrange("p h (i q) -> p i h q", q=SLOTS),
                    pair_ps[:, 2 * bank:2 * bank + 2, 0:ZC].rearrange("p i (h q) -> p i h q", q=SLOTS), ACT.Copy)

            extra = act.alloc_register("scalar_extra_passes")
            act.reg_mov(extra, 0)
            act.wait_ge(tab_in, 16)
            with act.Fori(0, TURNS) as turn:
                for k in range(BUFS):
                    s = turn * BUFS + k
                    passes = act.value_load(tab[0:1, bass.ds(s * NTAB + NC, 1)], min_val=1, max_val=MAXR)
                    for g in range(PAIRS):
                        act.wait_ge(pair_done, s * PAIRS + (g + 1))
                        read_pair(k, g % 2, g).then_inc(pair_read, 1)
                    act.wait_ge(slots_done, s + 1)
                    nc.scalar.activation(slot_half[:, :], slots_ps[0:NS, 0:C], ACT.Copy, scale=1.0 / SCALE).then_inc(half_ready, 1)
                    with act.If(passes > 1):
                        with act.Fori(1, passes):
                            n = act.snap(extra, min_val=0, max_val=S * MAXR)
                            for g in range(PAIRS):
                                act.wait_ge(xpair_done, n * PAIRS + (g + 1))
                                read_pair(k, 0, g).then_inc(xpair_read, 1)
                            act.wait_ge(xslots_done, n + 1)
                            nc.scalar.activation(slot_half[:, :], slots_ps[0:NS, 0:C], ACT.Copy, scale=1.0 / SCALE).then_inc(xhalf_ready, 1)
                            act.reg_add(extra, extra, 1)
            act.wait_ge(w_in, 16 * 5)
            with act.Fori(0, NB, 2) as b:
                relu(0, BLOCK, b)
                relu(1, BLOCK, b + 1)
            relu(0, NLAST, NB)

        @block.tensor
        def _(pe):
            extra = pe.alloc_register("tensor_extra_passes")
            pe.reg_mov(extra, 0)

            pe.wait_ge(consts, 1)
            pe.wait_ge(rel_T_ready, 1)
            for n in range(GROUPS):
                if n:
                    pe.wait_ge(turn_read, n)
                for bank, what in ((0, relT), (1, srcF)):
                    for t in range(n * PER, min(ADJ, (n + 1) * PER)):
                        at = (t - n * PER) * S
                        last = nc.tensor.transpose(pair_ps[:, bank, at:at + S], what[:, P * t:P * (t + 1)], ident[0:S, 0:S])
                    last.then_inc(turned, 1)
            pe.wait_ge(offs_ready, 1)
            nc.tensor.transpose(slots_ps[0:NS, 0:S], slotT[:, :, :].rearrange("s t q -> s (t q)"), ident[0:S, 0:S])
            nc.tensor.transpose(spread_ps[0:NS, 0:1], place_row[:, :, :].rearrange("o t q -> o (t q)"), ident[0:1, 0:1]).then_inc(turned, 1)
            pe.wait_ge(keys_ready, 1)
            pe.wait_ge(hl_ready, 1)

            def sum_windows(k, tiles, into=None):
                into = seg[k % 2] if into is None else into
                for t in tiles:
                    c = max(c for c in range(NC) if COL[c] <= t)
                    last = nc.tensor.matmul(into[0:C, W * c:W * (c + 1)], edges[k][:, t, :],
                                            hot[k % 2][:, t, :], start=(t == 0), stop=(t == TILES - 1),
                                            skip_group_check=True)
                return last

            def count_pair(buf, bank):
                for i in (0, 1):
                    last = nc.tensor.matmul(pair_ps[:, 2 * bank + i, 0:ZC], lo_hot[buf][:, i, :], z[buf][:, i, :], start=True, stop=True)
                return last

            def sum_slots(k):
                for h in range(NT):
                    last = nc.tensor.matmul(slots_ps[0:NS, 0:2 * C], adj[k % 2][:, h, :], hl[:, h, :],
                                            start=(h == 0), stop=(h == NT - 1))
                return last

            def spread_slots(into):
                return nc.tensor.matmul(into[0:C, 0:SPREAD], slot_sum[:, :], slot_hot[:, :], start=True, stop=True)

            def super_chunk(k, s, turn):
                passes = pe.value_load(tab[0:1, bass.ds(s * NTAB + NC, 1)], min_val=1, max_val=MAXR)
                pe.wait_ge(edges_in[k], (turn + 1) * (16 * NC))
                pe.wait_ge(hot_ready, s + 1)
                per = 1
                for g in range(PAIRS):
                    pe.wait_ge(z_ready, s * PAIRS + (g + 1))
                    if not (isinstance(s, int) and s * PAIRS + g < 2):
                        pe.wait_ge(pair_read, s * PAIRS + (g - 1))
                    count_pair(g % AHEAD, g % 2).then_inc(pair_done, 1)
                    sum_windows(k, range(per * g, per * (g + 1)))
                pe.wait_ge(pair_read, s * PAIRS + PAIRS)
                if not (isinstance(s, int) and s == 0):
                    pe.wait_ge(slots_ready, s)
                sum_slots(k).then_inc(slots_done, 1)
                sum_windows(k, range(per * PAIRS, ADJ))
                pe.wait_ge(gathered[k], (turn + 1) * (16 * (TILES - ADJ)))
                sum_windows(k, range(ADJ, TILES)).then_inc(seg_done, 1)
                pe.wait_ge(slots_ready, s + 1)
                spread_slots(spread_ps).then_inc(spread_done, 1)
                with pe.If(passes > 1):
                    with pe.Fori(1, passes):
                        n = pe.snap(extra, min_val=0, max_val=S * MAXR)
                        pe.wait_ge(xhot_ready, n + 1)
                        sum_windows(k, range(TILES), xseg_ps)
                        for g in range(PAIRS):
                            pe.wait_ge(xz_ready, n * PAIRS + (g + 1))
                            count_pair(AHEAD, 0).then_inc(xpair_done, 1)
                        pe.wait_ge(xpair_read, (n + 1) * PAIRS)
                        sum_slots(k).then_inc(xslots_done, 1)
                        pe.wait_ge(xslots_ready, n + 1)
                        spread_slots(xspread_ps).then_inc(xspread_done, 1)
                        pe.wait_ge(xseg_added, (n + 1) * (NC + 1))
                        pe.reg_add(extra, extra, 1)

            for k in range(BUFS):
                super_chunk(k, k, 0)
            with pe.Fori(1, TURNS) as turn:
                for k in range(BUFS):
                    super_chunk(k, turn * BUFS + k, turn)
            pe.wait_ge(agg_ready, 1)
            pe.wait_ge(w_in, 16 * 5)

            def hidden(k, n, b, first):
                if not first:
                    pe.wait_ge(hid_ready, b)
                for j in range(H):
                    last = nc.tensor.matmul(hid_ps[j][0:C, 0:n], w1_sb[:, j, :], accT[:, bass.ds(b * BLOCK, n)], start=True, stop=True)
                last.then_inc(hid_done, 1)

            def project(k, n, tile, g, b, reuse):
                if reuse:
                    pe.wait_ge(out_ready, tile - 1)
                for j in range(H):
                    last = nc.tensor.matmul(out_ps[g % 2][0:n, 0:C], hid[k][:, j, P * g:P * g + n], w2_sb[:, j, :],
                                            start=(j == 0), stop=(j == H - 1))
                last.then_inc(out_done, 1)

            def block_of(k, b, first):
                hidden(k, BLOCK, b, first)
                pe.wait_ge(hid_ready, b + 1)
                for g in range(G):
                    project(k, P, b * G + g, g, b, not (first and g < 2))

            block_of(0, 0, True)
            with pe.Fori(1, NB - 1, 2) as b:
                block_of(1, b, False)
                block_of(0, b + 1, False)
            block_of(1, NB - 1, False)
            hidden(0, NLAST, NB, False)
            pe.wait_ge(hid_ready, NB + 1)
            project(0, NLAST, NT - 1, 0, NB, True)


_INS = ["x", "src", "dst", "edge_attr_96", "L0_gnn_W1", "L0_gnn_b1", "L0_gnn_W2", "L0_gnn_b2", "L0_gnn_eps"]


def kernel(**inputs):
    import numpy as np
    import concourse.bacc as bacc
    from concourse.bass_utils import run_bass_kernel_spmd

    nc = bacc.Bacc("TRN2", target_bir_lowering=False, num_devices=1)
    arrays, args = {}, []
    for name in _INS:
        a = np.ascontiguousarray(inputs[name])
        arrays[f"in_{name}"] = a
        args.append(nc.dram_tensor(f"in_{name}", a.shape, mybir.dt.from_np(a.dtype), kind="ExternalInput").ap())
    out = nc.dram_tensor("out", inputs["x"].shape, F32, kind="ExternalOutput").ap()
    build(nc, *args, out)
    r = run_bass_kernel_spmd(nc, [arrays], core_ids=[0])
    return r.results[0]["out"]
```
